# Optimizing a Trainium2 kernel written in Bass

```python
import numpy as np
import jax
import jax.numpy as jnp

def _softmax(x, axis=-1):
    return jax.nn.softmax(x, axis=axis)

def _gelu(x):
    return jax.nn.gelu(x, approximate=True)

def _silu(x):
    return jax.nn.silu(x)

def _sigmoid(x):
    return jax.nn.sigmoid(x)

def _layernorm(x, axis=-1, eps=1e-05):
    m = jnp.mean(x, axis=axis, keepdims=True)
    v = jnp.var(x, axis=axis, keepdims=True)
    return (x - m) / jnp.sqrt(v + eps)

def _scatter_add(tgt, idx, src, axis=0):
    return tgt.at[idx].add(src)

def _segment_sum(src, seg, n):
    return jax.ops.segment_sum(src, seg, n)
kernel_name = 'mk_prb_d1_jaxref_r4_ad4026'

def setup_inputs(seed: int=0):
    np.random.seed(seed)
    _w = jnp.asarray

    def _L0_attn_setup():
        import jax, jax.numpy as jnp
        import numpy as np
        D = 512
        H = 8
        QK = D // 2
        FF = 2048
        CAP = 15.0
        EPS = 1e-06

        def _rmsnorm(x, w, eps=EPS):
            xf = x.astype(jnp.float32)
            var = jnp.mean(xf * xf, axis=-1, keepdims=True)
            return (w * xf * jax.lax.rsqrt(var + eps)).astype(x.dtype)

        def _soft_cap(x, cap=CAP):
            return cap * jnp.tanh(x / cap)

        def _mlstm_parallel(q, k, v, i_pre, f_pre):
            B, Hn, S, dqk = q.shape
            logfg = jax.nn.log_sigmoid(f_pre)
            Fcum = jnp.cumsum(logfg, axis=-1)
            Dmat = Fcum[..., :, None] - Fcum[..., None, :] + i_pre[..., None, :]
            causal = jnp.tril(jnp.ones((S, S), dtype=bool))
            Dmat = jnp.where(causal, Dmat, -jnp.inf)
            m = jnp.max(Dmat, axis=-1, keepdims=True)
            Smat = jnp.exp(Dmat - m)
            qk = jnp.einsum('bhsd,bhtd->bhst', q, k) / jnp.sqrt(jnp.float32(dqk))
            C = qk * Smat
            n = jnp.maximum(jnp.abs(jnp.sum(C, axis=-1, keepdims=True)), jnp.exp(-m))
            h = jnp.einsum('bhst,bhtd->bhsd', C / n, v)
            return h
        key = jax.random.key(seed)
        ks = jax.random.split(key, 17)
        sc = 0.02
        inp = {'x': jax.random.normal(ks[0], (2, 512, D), jnp.float32), 'norm1_w': jnp.ones((D,), jnp.float32), 'wq': jax.random.normal(ks[1], (D, QK), jnp.float32) * sc, 'wk': jax.random.normal(ks[2], (D, QK), jnp.float32) * sc, 'wv': jax.random.normal(ks[3], (D, D), jnp.float32) * sc, 'w_ig': jax.random.normal(ks[4], (D, H), jnp.float32) * sc, 'b_ig': jnp.zeros((H,), jnp.float32), 'w_fg': jax.random.normal(ks[5], (D, H), jnp.float32) * sc, 'b_fg': jnp.linspace(3.0, 6.0, H).astype(jnp.float32), 'w_og': jax.random.normal(ks[6], (D, D), jnp.float32) * sc, 'mh_w': jnp.ones((D,), jnp.float32), 'w_out': jax.random.normal(ks[7], (D, D), jnp.float32) * sc, 'norm2_w': jnp.ones((D,), jnp.float32), 'w_gate': jax.random.normal(ks[8], (D, FF), jnp.float32) * sc, 'w_up': jax.random.normal(ks[9], (D, FF), jnp.float32) * sc, 'w_down': jax.random.normal(ks[10], (FF, D), jnp.float32) * sc}
        return inp
    _L0_attn_in = _L0_attn_setup()

    def _L0_ffn_setup():
        import jax, jax.numpy as jnp
        import numpy as np
        HIDDEN = 512
        INTER = 1376
        LUT_SIZE = 16

        def _ghost_linear(x, idx, lut):
            w = lut[idx]
            return jnp.einsum('bsh,oh->bso', x, w)
        key = jax.random.key(seed)
        k_x, k_lut, k_g, k_u, k_d = jax.random.split(key, 5)
        x = jax.random.normal(k_x, (2, 1024, HIDDEN), dtype=jnp.float32)
        lut = jax.random.normal(k_lut, (LUT_SIZE,), dtype=jnp.float32) * 0.02
        gate_idx = jax.random.randint(k_g, (INTER, HIDDEN), 0, LUT_SIZE, dtype=jnp.int32)
        up_idx = jax.random.randint(k_u, (INTER, HIDDEN), 0, LUT_SIZE, dtype=jnp.int32)
        down_idx = jax.random.randint(k_d, (HIDDEN, INTER), 0, LUT_SIZE, dtype=jnp.int32)
        return {'x': x, 'lut': lut, 'gate_idx': gate_idx, 'up_idx': up_idx, 'down_idx': down_idx}
    _L0_ffn_in = _L0_ffn_setup()
    _d = {'L0_attn_x': _L0_attn_in['x'], 'L0_attn_norm1_w': _L0_attn_in['norm1_w'], 'L0_attn_wq': _L0_attn_in['wq'], 'L0_attn_wk': _L0_attn_in['wk'], 'L0_attn_wv': _L0_attn_in['wv'], 'L0_attn_w_ig': _L0_attn_in['w_ig'], 'L0_attn_b_ig': _L0_attn_in['b_ig'], 'L0_attn_w_fg': _L0_attn_in['w_fg'], 'L0_attn_b_fg': _L0_attn_in['b_fg'], 'L0_attn_w_og': _L0_attn_in['w_og'], 'L0_attn_mh_w': _L0_attn_in['mh_w'], 'L0_attn_w_out': _L0_attn_in['w_out'], 'L0_attn_norm2_w': _L0_attn_in['norm2_w'], 'L0_attn_w_gate': _L0_attn_in['w_gate'], 'L0_attn_w_up': _L0_attn_in['w_up'], 'L0_attn_w_down': _L0_attn_in['w_down'], 'L0_ffn_lut': _L0_ffn_in['lut'], 'L0_ffn_gate_idx': _L0_ffn_in['gate_idx'], 'L0_ffn_up_idx': _L0_ffn_in['up_idx'], 'L0_ffn_down_idx': _L0_ffn_in['down_idx']}
    _x0 = _d['L0_attn_x']
    _d['L0_attn_x'] = jax.random.normal(jax.random.fold_in(jax.random.key(seed), 1), (4, 1024, 512), dtype=_x0.dtype)
    del _x0
    return _d

def reference(L0_attn_x, L0_attn_norm1_w, L0_attn_wq, L0_attn_wk, L0_attn_wv, L0_attn_w_ig, L0_attn_b_ig, L0_attn_w_fg, L0_attn_b_fg, L0_attn_w_og, L0_attn_mh_w, L0_attn_w_out, L0_attn_norm2_w, L0_attn_w_gate, L0_attn_w_up, L0_attn_w_down, L0_ffn_lut, L0_ffn_gate_idx, L0_ffn_up_idx, L0_ffn_down_idx):

    def _L0_attn_ref(x, norm1_w, wq, wk, wv, w_ig, b_ig, w_fg, b_fg, w_og, mh_w, w_out, norm2_w, w_gate, w_up, w_down):
        import jax, jax.numpy as jnp
        import numpy as np
        D = 512
        H = 8
        QK = D // 2
        FF = 2048
        CAP = 15.0
        EPS = 1e-06

        def _rmsnorm(x, w, eps=EPS):
            xf = x.astype(jnp.float32)
            var = jnp.mean(xf * xf, axis=-1, keepdims=True)
            return (w * xf * jax.lax.rsqrt(var + eps)).astype(x.dtype)

        def _soft_cap(x, cap=CAP):
            return cap * jnp.tanh(x / cap)

        def _mlstm_parallel(q, k, v, i_pre, f_pre):
            B, Hn, S, dqk = q.shape
            logfg = jax.nn.log_sigmoid(f_pre)
            Fcum = jnp.cumsum(logfg, axis=-1)
            Dmat = Fcum[..., :, None] - Fcum[..., None, :] + i_pre[..., None, :]
            causal = jnp.tril(jnp.ones((S, S), dtype=bool))
            Dmat = jnp.where(causal, Dmat, -jnp.inf)
            m = jnp.max(Dmat, axis=-1, keepdims=True)
            Smat = jnp.exp(Dmat - m)
            qk = jnp.einsum('bhsd,bhtd->bhst', q, k) / jnp.sqrt(jnp.float32(dqk))
            C = qk * Smat
            n = jnp.maximum(jnp.abs(jnp.sum(C, axis=-1, keepdims=True)), jnp.exp(-m))
            h = jnp.einsum('bhst,bhtd->bhsd', C / n, v)
            return h
        B, S, _ = x.shape
        dqk, dv = (QK // H, D // H)
        h_in = _rmsnorm(x, norm1_w)
        q = (h_in @ wq).reshape(B, S, H, dqk).transpose(0, 2, 1, 3)
        k = (h_in @ wk).reshape(B, S, H, dqk).transpose(0, 2, 1, 3)
        v = (h_in @ wv).reshape(B, S, H, dv).transpose(0, 2, 1, 3)
        o_pre = h_in @ w_og
        i_pre = _soft_cap(h_in @ w_ig + b_ig).transpose(0, 2, 1)
        f_pre = _soft_cap(h_in @ w_fg + b_fg).transpose(0, 2, 1)
        h = _mlstm_parallel(q, k, v, i_pre, f_pre)
        h = h.transpose(0, 2, 1, 3)
        hf = h.astype(jnp.float32)
        var = jnp.mean(hf * hf, axis=-1, keepdims=True)
        h_norm = hf * jax.lax.rsqrt(var + EPS) * mh_w.reshape(H, dv)
        h_norm = h_norm.reshape(B, S, D)
        h_out = jax.nn.sigmoid(o_pre) * h_norm
        x1 = x + h_out @ w_out
        h2 = _rmsnorm(x1, norm2_w)
        mlp = jax.nn.silu(h2 @ w_gate) * (h2 @ w_up) @ w_down
        return x1 + mlp

    def _L0_ffn_ref(x, lut, gate_idx, up_idx, down_idx):
        import jax, jax.numpy as jnp
        import numpy as np
        HIDDEN = 512
        INTER = 1376
        LUT_SIZE = 16

        def _ghost_linear(x, idx, lut):
            w = lut[idx]
            return jnp.einsum('bsh,oh->bso', x, w)
        gate = _ghost_linear(x, gate_idx, lut)
        up = _ghost_linear(x, up_idx, lut)
        h = jax.nn.silu(gate) * up
        return _ghost_linear(h, down_idx, lut)
    x = L0_attn_x
    xn = _layernorm(x, axis=-1)
    x = x + _L0_attn_ref(xn, L0_attn_norm1_w, L0_attn_wq, L0_attn_wk, L0_attn_wv, L0_attn_w_ig, L0_attn_b_ig, L0_attn_w_fg, L0_attn_b_fg, L0_attn_w_og, L0_attn_mh_w, L0_attn_w_out, L0_attn_norm2_w, L0_attn_w_gate, L0_attn_w_up, L0_attn_w_down) + _L0_ffn_ref(xn, L0_ffn_lut, L0_ffn_gate_idx, L0_ffn_up_idx, L0_ffn_down_idx)
    return x

_drawn_inputs = setup_inputs


def setup_inputs(seed=0):
    import zlib

    import numpy as np

    out = dict(_drawn_inputs(seed))
    spreads = {'L0_attn_norm1_w': (1.0, 0.2),
     'L0_attn_b_ig': (0.0, 0.8),
     'L0_attn_mh_w': (1.0, 0.6),
     'L0_attn_norm2_w': (1.0, 0.6)}
    factors = {'L0_attn_w_fg': 8.0}
    for name, (base, spread) in spreads.items():
        noise = np.random.default_rng([zlib.crc32(name.encode()), seed]).standard_normal(out[name].shape)
        drawn = base * np.exp(spread * noise) if base else spread * noise
        out[name] = jnp.asarray(drawn.astype(out[name].dtype))
    for name, factor in factors.items():
        out[name] = (out[name] * factor).astype(out[name].dtype)
    return out
```

```python
import concourse.bass as bass
from concourse import mybir
from contextlib import ExitStack
import numpy as np

P = 128
D = 512
KT = D // P
H = 8
DQ = 32
DV = 64
VS = DV + 1
G = 2
HG = H // G
BATCH, SEQ = 4, 1024
TOK = 512
NB = TOK // P
HALVES = SEQ // TOK
FF, INTER, LUT = 2048, 1376, 16
NF = -(-INTER // P)
NM = FF // P
NT = NF + NM
INTER_PAD = NF * P
GU = 2 * KT * P
UNITS = NB * G
LOOPED = 10
CAP = 15.0
EPS_LN, EPS_RMS = 1e-5, 1e-6
FAR = -1e30
MASKED = -1e4
RW = 72
QSCALE = float(DQ) ** -0.5


class Steps:

    def __init__(self, sem, per_pass, names, credit=0, ahead=0):
        self.sem, self.per_pass, self.names, self.credit, self.ahead = sem, per_pass, names, credit, ahead

    def of(self, at, k, name):
        n = len(self.names)
        step = self.names.index(name) + 1
        b, half = at
        const = (half * self.per_pass) * n + step + self.credit + self.ahead * n
        if isinstance(k, int):
            const, k = const + k * n, None
        value = b * (HALVES * self.per_pass * n) + const
        return value if k is None else value + k * n

    def before(self, at):
        return self.of(at, 0, self.names[0]) - 1


def program(nc, x, w_attn, w_gates, norm1, b_gates, mh_w, norm2, w_gu, w_dn, lut, idx, out):
    f32, f32r, i32 = mybir.dt.float32, mybir.dt.float32r, mybir.dt.int32
    ALU, ACT, AX = mybir.AluOpType, mybir.ActivationFunctionType, mybir.AxisListType
    ctx = ExitStack()
    with ctx:
        def sb(name, shape, dt=f32):
            return ctx.enter_context(nc.sbuf_tensor(name, shape, dt))

        def sem(name):
            return ctx.enter_context(nc.semaphore(name))

        ffn = nc.dram_tensor("ffn_weights", (NF, P, GU + D), f32, kind="Internal").ap()

        WA = [sb(f"attn_w_{s}", [P, 4, KT, D], f32r) for s in ("hi", "lo")]
        WG = [sb(f"gates_w_{s}", [P, KT, 2 * H], f32r) for s in ("hi", "lo")]
        raw_gu = sb("raw_gu", [P, 2, GU])
        raw_dn = sb("raw_dn", [P, D])
        WGU = [sb(f"gu_{s}", [P, 2, GU], f32r) for s in ("hi", "lo")]
        WDN = [sb(f"dn_{s}", [P, 2, D], f32r) for s in ("hi", "lo")]
        XN = [sb(f"xn_{i}", [P, NB, D]) for i in range(2)]
        XT = [sb(f"xT_{s}", [P, KT, TOK], f32r) for s in ("hi", "lo")]
        HT = [sb(f"hT_{s}", [P, KT, TOK], f32r) for s in ("hi", "lo")]
        th = sb("th", [P, TOK])
        hm = sb("hm", [P, TOK])
        HH = [sb(f"hidden_{s}", [P, TOK], f32r) for s in ("hi", "lo")]
        qkT = sb("qkT", [P, 2, G, TOK])
        kn = sb("kn", [P, NB, H * DQ])
        va = sb("va", [P, NB * H * VS + P - VS])
        qbd = sb("qbd", [P, HG, P])
        ar = sb("ar", [P, HG, P])
        ex = sb("ex", [P, HG, P])
        ct = sb("ct", [P, HG, P])
        vw = sb("vw", [P, 2, HG, VS])
        tt = sb("tt", [P, HG, VS])
        hr = sb("hr", [P, H, VS])
        hn = sb("hn", [P, H, DV])
        kv = sb("kv", [P, G, HG, VS])
        MX = sb("MX", [P, H, P], f32r)
        AL = sb("AL", [P, TOK], f32r)
        mhl = sb("mhl", [P, TOK])
        mx = sb("mx", [H, 1 + TOK])
        gcar = sb("gcar", [H, 1])
        rn = sb("rn", [P, NB * RW + G * NB])
        gn = sb("gn", [P, NB, 2 * H])
        gn2 = sb("gn2", [P, NB, 2 * H])
        gt = sb("gt", [P, NB, 40])
        tf = sb("tf", [P, NB, H])
        ef = sb("ef", [P, NB, H])
        st6 = sb("st6", [P, NB, 6])
        mv = sb("mv", [P, NB, 2])
        ve = sb("ve", [P, NB])
        rs = sb("rs", [P, NB])
        r1 = [sb(f"r1_{i}", [P, 3, NB]) for i in range(2)]
        nm = sb("nm", [P, H])
        sm = sb("sm", [P, H])
        rh = sb("rh", [P, H])
        ident = sb("ident", [P, P])
        maskd = sb("maskd", [P, P])
        bdm = sb("bdm", [P, HG])
        hm32 = sb("hm32", [P, 32])
        rep = sb("rep", [H, H, DQ])
        mhb = sb("mhb", [P, D])
        n1 = sb("n1", [P, KT])
        n2 = sb("n2", [P, KT])
        gb = sb("gb", [P, 2 * H])
        one = sb("one", [H, 1])
        half_pow = sb("half_pow", [P, H])
        lt = sb("lt", [P, LUT])
        ld = sb("ld", [P, LUT // 2])

        def og(half):
            return XN[1 - half]

        def rows(half):
            o = XN[1 - half]
            return o[0:H, 3, :], o[0:H, 2, :], o[0:H, 1, :], o[:, 0, :]
        gts = ar[0:2 * H, :, :].rearrange("p a b -> p (a b)")
        ah = hn[0:H, :, :].rearrange("p a b -> p (a b)").bitcast(f32r)
        rwe = ex[:, :, :].rearrange("p a b -> p (a b)")
        qn = vw[:, :, :, :].rearrange("p a b c -> p (a b c)")[:, 0:2 * H * DQ].rearrange("p (a n) -> p a n", a=2)
        to = [th, hm]
        xr = qkT[:, :, :, :].rearrange("p a b n -> p (a b n)").rearrange("p (i n) -> p i n", i=NB)
        h2_rows = [ex[:, :, :].rearrange("p a b -> p (a b)"), hn[:, :, :].rearrange("p a b -> p (a b)"),
                   ar[:, :, :].rearrange("p a b -> p (a b)"), ex[:, :, :].rearrange("p a b -> p (a b)")]
        sq = ar[:, :, :].rearrange("p a b -> p (a b)").rearrange("p (h d) -> p h d", h=H)

        ACC = [ctx.enter_context(nc.psum_tensor(f"acc{i}", [P, D], f32)) for i in range(NB)]
        GB = ctx.enter_context(nc.psum_tensor("gate_bank", [P, TOK], f32))
        UB = ctx.enter_context(nc.psum_tensor("up_bank", [P, TOK], f32))
        A = ctx.enter_context(nc.psum_tensor("bank_a", [P, TOK], f32))
        B = ctx.enter_context(nc.psum_tensor("bank_b", [P, TOK], f32))
        AB = [B, A]

        ld_const = sem("ld_const")
        ld_gu = [sem(f"ld_gu{i}") for i in range(2)]
        ld_dn = sem("ld_dn")
        ld_x = [sem(f"ld_x{i}") for i in range(2)]
        ld_xr = sem("ld_xr")
        ld_w = [sem(f"ld_w{i}") for i in range(4)]
        ld_idx = [sem(f"ld_idx{i}") for i in range(3)]
        st_w = [sem(f"st_w{i}") for i in range(3)]
        st_zero = sem("st_zero")
        look_act = sem("look_act")
        look_vec = sem("look_vec")
        st_out = [sem(f"st_out{i}") for i in range(2)]
        out_left = sem("out_left")
        pool_const = sem("pool_const")
        vec_const = sem("vec_const")
        act_pre = sem("act_pre")
        vec_pre = sem("vec_pre")
        pool_pre = sem("pool_pre")
        pe_passed = sem("pe_passed")
        vec_passed = sem("vec_passed")
        pe_gates = Steps(sem("pe_gates"), 1, ["logits", "natural", "rows", "factors"])
        pe_qk = Steps(sem("pe_qk"), NB, ["done"])
        pe_qkT = Steps(sem("pe_qkT"), NB, ["done"])
        pe_v = Steps(sem("pe_v"), NB, ["done"])
        pe_o = Steps(sem("pe_o"), NB, ["done"])
        pe_unit = Steps(sem("pe_unit"), UNITS, ["exponents", "scores", "values", "state"], credit=1)
        pe_hoT = Steps(sem("pe_hoT"), NB, ["done"])
        pe_out = Steps(sem("pe_out"), NB, ["done"])
        pe_h2T = Steps(sem("pe_h2T"), NB, ["done"])
        pe_xT = Steps(sem("pe_xT"), NB, ["done"], ahead=NB)
        pe_gate = Steps(sem("pe_gate"), NT, ["done"])
        pe_up = Steps(sem("pe_up"), NT, ["done"], credit=2)
        pe_down = Steps(sem("pe_down"), NT, ["done"], credit=2)
        act_gates = Steps(sem("act_gates"), 1, ["logits", "tanh_i", "tanh_f", "exp", "log", "f_rows", "a_hi", "exps0", "exps1", "exps"])
        act_qk = Steps(sem("act_qk"), NB, ["q", "k"])
        act_qkT = Steps(sem("act_qkT"), NB, ["q", "k"])
        act_v = Steps(sem("act_v"), NB, ["done"])
        act_o = Steps(sem("act_o"), NB, ["done"])
        act_unit = Steps(sem("act_unit"), UNITS, ["exp"])
        act_hoT = Steps(sem("act_hoT"), NB, ["hi"])
        act_h2T = Steps(sem("act_h2T"), NB, ["hi"])
        act_xT = Steps(sem("act_xT"), NB, ["hi"], ahead=NB)
        act_tanh = Steps(sem("act_tanh"), NT, ["done"])
        act_hid = Steps(sem("act_hid"), NT, ["hi"])
        act_wgu = Steps(sem("act_wgu"), NT, ["hi"])
        act_wdn = Steps(sem("act_wdn"), NT, ["hi"])
        ROWS = ["scaled", "biased", "m0", "g0", "cum", "a", "a_hi", "a_lo", "max", "m_hi", "m_lo",
                "inter", "keys", "bound", "carry", "factors"]
        vec_rows = Steps(sem("vec_rows"), 1, ROWS)
        vec_o = Steps(sem("vec_o"), NB, ["done"])
        vec_unit = Steps(sem("vec_unit"), UNITS, ["masked", "weights", "before", "heads", "update", "state"])
        vec_norm = Steps(sem("vec_norm"), NB, ["size", "floor", "inverse", "divided", "squares", "sums", "mean", "scaled", "gated"])
        vec_hoT = Steps(sem("vec_hoT"), NB, ["lo"])
        vec_x1 = Steps(sem("vec_x1"), NB, ["x1", "stats", "mv", "ms", "ms2"])
        vec_h2 = Steps(sem("vec_h2"), NB, ["done"])
        vec_h2S = Steps(sem("vec_h2S"), NB, ["scaled"])
        vec_h2T = Steps(sem("vec_h2T"), NB, ["lo"], credit=1)
        vec_res = Steps(sem("vec_res"), NB, ["done"], credit=1)
        LN = [f"stats{i}" for i in range(NB)] + [f"mv{i}" for i in range(NB)] + ["ve", "r2", "vr", "ve1", "r1q", "r1h"] \
            + [f"xn{i}" for i in range(NB)]
        vec_ln = Steps(sem("vec_ln"), 1, LN, ahead=1)
        vec_xT = Steps(sem("vec_xT"), NB, ["lo"], ahead=NB)
        vec_gate = Steps(sem("vec_gate"), NT, ["done"], credit=1)
        vec_hm = Steps(sem("vec_hm"), NT, ["done"], credit=1)
        vec_out = Steps(sem("vec_out"), NB, ["done"], credit=1)
        pool_mx = Steps(sem("pool_mx"), NB, ["done"], credit=1)
        act_qbd = Steps(sem("act_qbd"), UNITS, ["h0", "h1", "h2", "h3"])
        pool_vw = Steps(sem("pool_vw"), UNITS, ["done"])
        pool_norm = Steps(sem("pool_norm"), NB, ["root"])
        pool_x1 = Steps(sem("pool_x1"), NB, ["root"])
        pool_ln = Steps(sem("pool_ln"), 1, ["root", "root1"], ahead=1)
        pool_hid = Steps(sem("pool_hid"), NT, ["lo"], credit=1)
        pool_wgu = Steps(sem("pool_wgu"), NT, ["lo"], credit=2, ahead=0)
        pool_wdn = Steps(sem("pool_wdn"), NT, ["lo"], credit=1)

        MUX = [(0, 0, 1, 1), (2, 0, 3, 1), (4, 0, 5, 1), (6, 0, 7, 1), (0, 1, 2, 2), (4, 1, 6, 2), (0, 2, 4, 3)]
        POOL_CONSTS = 13
        LOOK_C = 4 + len(MUX)
        LOOK_V = 3 * LOOK_C
        LOOK_CREDIT = LOOK_V + 1
        LOOK_NEEDS = [max([n + 1 for n, o in enumerate(MUX[:m]) if {o[0], o[2]} & {e[0], e[2]}], default=0)
                      for m, e in enumerate(MUX)]
        LOOK_FREES = {k: 4 + 1 + max(n for n, m in enumerate(MUX) if k in (m[0], m[2])) for k in range(LUT // 2)}
        BANKS = [None, A, B, GB, UB, ACC[0], ACC[1], ACC[2]]
        wbuf = [th[:], hm[:], raw_dn[:]]
        fl = "p a b -> p (a b)"
        b0 = [qbd[:, :, :].rearrange(fl), hn[:, :, :].rearrange(fl), kn[:, 0:2, :].rearrange(fl)]
        bits = [ar[:, :, :].rearrange(fl), ex[:, :, :].rearrange(fl), ct[:, :, :].rearrange(fl)]
        ixb = [qkT[:, z, g, :].bitcast(i32) for z, g in ((0, 0), (0, 1), (1, 0))]
        raw_w = [raw_gu[:, 0, :], raw_gu[:, 1, :]] + [XN[1][:, z:z + 2, :].rearrange("p k n -> p (k n)") for z in (0, 2)]
        zero_rows = qkT[:, 1, 1, :]

        PRE = (0, -1)

        def wait(e, steps, at, k, name="done"):
            e.wait_ge(steps.sem, steps.of(at, k, name))

        block = ctx.enter_context(nc.Block())

        @block.sync
        def _(sp):
            sp.sem_inc(out_left, 1)
            for dst, src in ((n1[:], norm1), (n2[:], norm2), (gb[:], b_gates), (mhb[:], mh_w), (lt[:], lut)):
                sp.dma_start(dst, src).then_inc(ld_const, 16)
            sp.dma_start(XN[0][:], x[0:TOK, :].rearrange("(i p) n -> p i n", p=P)).then_inc(ld_x[0], 16)
            for m in range(8):
                if m >= 4:
                    sp.wait_ge(pool_pre, m - 3)
                sp.dma_start(raw_w[m % 4], w_attn[m]).then_inc(ld_w[m % 4], 16)
            sp.wait_ge(pool_pre, 5)
            sp.dma_start(raw_w[0][:, 0:KT * 2 * H], w_gates).then_inc(ld_w[0], 16)
            sp.wait_ge(pool_pre, 9)

            def load_gu(at, k, slot, src):
                sp.wait_ge(pool_wgu.sem, pool_wgu.of(at, k, "lo") - 2)
                sp.dma_start(raw_gu[:, slot, :], src).then_inc(ld_gu[slot], 16)

            def load_dn(at, k, src):
                sp.wait_ge(pool_wdn.sem, pool_wdn.of(at, k, "lo") - 1)
                sp.dma_start(raw_dn[:], src).then_inc(ld_dn, 16)

            with sp.Fori(0, NF) as t:
                for c in range(3):
                    sp.wait_ge(look_vec, t * LOOK_V + (c * LOOK_C + LOOK_CREDIT + 3 - LOOK_V))
                    sp.dma_start(ixb[c], idx[bass.ds(t, 1), :, c * D:(c + 1) * D].rearrange("a p n -> (a p) n"))\
                        .then_inc(ld_idx[c], 16)
            sp.wait_ge(look_vec, NF * LOOK_V + LOOK_CREDIT + 3 - LOOK_V)
            sp.dma_start(ixb[0], idx[0, :, 0:D]).then_inc(ld_idx[0], 16)
            for c in range(3):
                sp.wait_ge(st_w[c], 16 * NF)
            sp.wait_ge(st_zero, 16)
            load_gu((0, 0), 0, 0, ffn[0, :, 0:GU])
            with sp.Fori(0, BATCH) as b:
                for half in range(HALVES):
                    at = (b, half)
                    for t in range(NF):
                        nxt = ffn[t + 1, :, 0:GU] if t + 1 < NF else w_gu[0]
                        load_gu(at, t + 1, (half * NT + t + 1) % 2, nxt)
                        load_dn(at, t, ffn[t, :, GU:])
                        if t == NF - 1:
                            wait(sp, pe_unit, at, UNITS - 1, "values")
                            sp.dma_start(xr[:, :, :], x[bass.ds((b * HALVES + half) * TOK, TOK), :]
                                         .rearrange("(i p) n -> p i n", p=P)).then_inc(ld_xr, 16)
                    wait(sp, vec_norm, at, NB - 1, "gated")
                    nxt_row = ((b * HALVES + half + 1) % (BATCH * HALVES)) * TOK
                    sp.dma_start(XN[1 - half][:], x[bass.ds(nxt_row, TOK), :].rearrange("(i p) n -> p i n", p=P))\
                        .then_inc(ld_x[1 - half], 16)
                    with sp.Fori(0, NM // 2 - 1) as i:
                        for q in range(2):
                            t = NF + q
                            load_gu(at, i * 2 + (t + 1), (half * NT + t + 1) % 2,
                                    w_gu[bass.ds(i * 2 + (q + 1), 1), :, :].rearrange("a p n -> (a p) n"))
                            load_dn(at, i * 2 + t, w_dn[bass.ds(i * 2 + q, 1), :, :].rearrange("a p n -> (a p) n"))
                    for t in range(NT - 2, NT):
                        nxt = w_gu[t + 1 - NF] if t + 1 < NT else ffn[0, :, 0:GU]
                        load_gu(at, t + 1, (half * NT + t + 1) % 2, nxt)
                        load_dn(at, t, w_dn[t - NF])
                    if half:
                        sp.wait_ge(st_out[1], b * (16 * NB) + 16 * NB)
                        sp.sem_inc(out_left, 1)
            sp.wait_ge(ld_gu[0], 16 * (BATCH * NT + 1))
            sp.wait_ge(ld_x[0], 16 * (BATCH + 1))

        @block.tensor
        def _(pe):
            pe.sem_inc(pe_unit.sem, 1)
            pe.sem_inc(pe_up.sem, 2)
            pe.sem_inc(pe_down.sem, 2)

            def split(dst, lhs, rhs, first=True, last=True):
                for k, (l, r) in enumerate(zip(lhs, rhs)):
                    for n, (a, c) in enumerate(((0, 0), (0, 1), (1, 0))):
                        mm = pe.matmul(dst, l[a], r[c], start=first and k == 0 and n == 0,
                                       stop=last and k == len(lhs) - 1 and n == 2)
                return mm

            def pair(t, *ix):
                return (t[0][ix], t[1][ix])

            S_ = slice(None)

            def toks(i):
                return slice(i * P, (i + 1) * P)

            def proj(at, n):
                kind, i = n // NB, n % NB
                if n < 2:
                    wait(pe, vec_xT, (at[0], at[1] - 1), NB - 2 + n, "lo")
                elif n < NB + 2:
                    wait(pe, act_qk, at, n - 2, "k")
                elif n < 2 * NB + 2:
                    wait(pe, act_v, at, n - 2 - NB)
                else:
                    wait(pe, act_o, at, n - 2 - 2 * NB)
                split(AB[n % 2][:], [pair(XT, S_, k, toks(i)) for k in range(KT)],
                      [pair(WA, S_, kind, k, S_) for k in range(KT)]).then_inc((pe_qk, pe_v, pe_o)[kind].sem, 1)

            def transposes(dst, srcs, stage):
                for k, s in enumerate(srcs):
                    mm = pe.transpose(dst[:, k * P:(k + 1) * P], s, ident[:])
                mm.then_inc(stage.sem, 1)

            def q_k_T(at, i):
                wait(pe, act_qk, at, i, "k")
                if i:
                    wait(pe, act_qkT, at, i - 1, "k")
                else:
                    wait(pe, vec_gate, (at[0], at[1] - 1), NT - 1)
                transposes(GB, [qn[:, i % 2, g * P:(g + 1) * P] for g in range(G)]
                           + [kn[:, i, g * P:(g + 1) * P] for g in range(G)], pe_qkT)

            def unit_1(at, u):
                j, g = u // G, u % G
                wait(pe, pool_mx, at, j)
                if u == 0:
                    wait(pe, act_gates, at, 0, "a_hi")
                    wait(pe, vec_rows, at, 0, "factors")
                    wait(pe, act_o, at, NB - 1)
                elif u >= 4 and u % 2 == 1 or u == 3:
                    wait(pe, vec_hoT, at, u // 2 - 1, "lo")
                else:
                    wait(pe, vec_unit, at, u - 1, "heads")
                pe.matmul(A[:], AL[:, toks(j)], MX[:, g * HG:(g + 1) * HG, :], start=True, stop=True)\
                    .then_inc(pe_unit.sem, 1)
                wait(pe, act_qbd, at, u, "h3")
                wait(pe, act_qkT, at, NB - 1, "k")
                if u:
                    wait(pe, vec_unit, at, u - 1, "update")
                pe.matmul(B[:], qkT[:, 1, g, toks(j)], qbd[:, :, :], start=True, stop=True)\
                    .then_inc(pe_unit.sem, 1)

            def unit_2(at, u):
                j, g = u // G, u % G
                wait(pe, vec_unit, at, u, "weights")
                if u >= 2:
                    wait(pe, vec_unit, at, u - 2, "state")
                pe.matmul(B[:, 0:HG * VS], qkT[:, 0, g, toks(j)], kv[:, g, :, :], start=True, stop=True)
                for h in range(HG):
                    c = (j * H + g * HG + h) * VS
                    mm = pe.matmul(A[:, h * P:(h + 1) * P], ct[:, h, :], va[:, c:c + P], start=True, stop=True)
                mm.then_inc(pe_unit.sem, 1)

            def unit_3(at, u):
                j, g = u // G, u % G
                wait(pe, vec_unit, at, u, "before")
                wait(pe, pool_vw, at, u)
                pe.matmul(B[:, 0:HG * VS], kn[:, j, g * P:(g + 1) * P], vw[:, u % 2, :, :], start=True, stop=True)\
                    .then_inc(pe_unit.sem, 1)

            def ho_T(at, i):
                wait(pe, vec_norm, at, i, "gated")
                wait(pe, vec_unit, at, min(2 * i + 2, UNITS - 1), "heads")
                f = hn[:, :, :].rearrange("p h d -> p (h d)")
                transposes(A, [f[:, k * P:(k + 1) * P] for k in range(KT)], pe_hoT)

            def out_proj(at, i):
                wait(pe, vec_hoT, at, NB - 1, "lo")
                if i == 0:
                    wait(pe, vec_unit, at, UNITS - 1, "update")
                elif i >= 2:
                    wait(pe, vec_x1, at, i - 2, "x1")
                split(AB[i % 2][:], [pair(HT, S_, k, toks(i)) for k in range(KT)],
                      [pair(WA, S_, 3, k, S_) for k in range(KT)]).then_inc(pe_out.sem, 1)

            def h2_T(at, i):
                wait(pe, vec_h2, at, i)
                if i < 2:
                    wait(pe, vec_x1, at, i + 2, "x1")
                else:
                    wait(pe, vec_h2S, at, i - 2, "scaled")
                f = h2_rows[i]
                transposes(AB[i % 2], [f[:, k * P:(k + 1) * P] for k in range(KT)], pe_h2T)

            def x_T(at, i, src, first=False):
                wait(pe, vec_ln, at, 0, f"xn{i}")
                if i >= 2:
                    wait(pe, vec_xT, at, i - 2, "lo")
                elif not first:
                    wait(pe, vec_h2S, at, i + 2, "scaled")
                transposes(AB[i % 2], [src[:, i, k * P:(k + 1) * P] for k in range(KT)], pe_xT)

            def gate(at, t, slot, act, ready=None):
                wait(pe, pool_wgu, at, t, "lo")
                gate_free(at, t)
                split(GB[:], [pair(WGU, S_, slot, slice(k * P, (k + 1) * P)) for k in range(KT)],
                      [pair(act, S_, k, S_) for k in range(KT)]).then_inc(pe_gate.sem, 1)

            def gate_free(at, t):
                if isinstance(t, int) and t == 0:
                    wait(pe, act_qkT, at, NB - 1, "k")
                else:
                    wait(pe, vec_gate, at, t + -1)

            def up(at, t, slot, act):
                if isinstance(t, int) and t == 0:
                    wait(pe, vec_rows, at, 0, "factors")
                else:
                    wait(pe, vec_hm, at, t + -1)
                split(UB[:], [pair(WGU, S_, slot, slice((KT + k) * P, (KT + k + 1) * P)) for k in range(KT)],
                      [pair(act, S_, k, S_) for k in range(KT)]).then_inc(pe_up.sem, 1)

            def down(at, t, slot, first=False, last=False):
                wait(pe, pool_wdn, at, t, "lo")
                wait(pe, pool_hid, at, t, "lo")
                for i in range(NB):
                    mm = split(ACC[i][:], [pair(HH, S_, toks(i))], [pair(WDN, S_, slot, S_)], first=first, last=last)
                mm.then_inc(pe_down.sem, 1)

            pe.wait_ge(pool_const, POOL_CONSTS)
            for i in range(NB):
                x_T(PRE, i, XN[0], first=True)
            pe.wait_ge(look_vec, LOOK_CREDIT + NF * LOOK_V)
            with pe.Fori(0, BATCH) as b:
                for half in range(HALVES):
                    at = (b, half)
                    before = (b, half - 1)

                    def slot(t):
                        return (half * NT + t) % 2

                    pe.wait_ge(pool_pre, 9)
                    wait(pe, vec_xT, before, NB - 1, "lo")
                    pe.wait_ge(vec_hm.sem, vec_hm.before(at))
                    split(UB[0:2 * H, :], [pair(WG, S_, k, S_) for k in range(KT)],
                          [pair(XT, S_, k, S_) for k in range(KT)]).then_inc(pe_gates.sem, 1)
                    proj(at, 0)
                    wait(pe, act_gates, at, 0, "logits")
                    pe.sem_inc(pe_passed, 1)
                    for i in range(NB):
                        mm = pe.transpose(UB[:, i * 2 * H:(i + 1) * 2 * H], gts[:, toks(i)], ident[0:2 * H, 0:2 * H])
                    mm.then_inc(pe_gates.sem, 1)
                    proj(at, 1)
                    q_k_T(at, 0)
                    proj(at, 2)
                    q_k_T(at, 1)
                    proj(at, 3)
                    wait(pe, act_gates, at, 0, "log")
                    pe.sem_inc(pe_passed, 1)
                    for i in range(NB):
                        mm = pe.transpose(UB[0:40, toks(i)], gt[:, i, :], ident[:])
                    mm.then_inc(pe_gates.sem, 1)
                    q_k_T(at, 2)
                    proj(at, 4)
                    q_k_T(at, 3)
                    for n in range(5, 9):
                        proj(at, n)
                    wait(pe, act_gates, at, 0, "exps")
                    wait(pe, vec_rows, at, 0, "a")
                    pe.sem_inc(pe_passed, 1)
                    for i in range(NB):
                        pe.transpose(UB[:, i * RW:(i + 1) * RW], rwe[0:RW, toks(i)], ident[0:RW, 0:RW])
                    for g in range(G):
                        c = NB * RW + g * NB
                        mm = pe.matmul(UB[:, c:c + NB], rep[:, g * HG:(g + 1) * HG, :], rwe[0:H, P - 1::P],
                                       start=True, stop=True)
                    mm.then_inc(pe_gates.sem, 1)
                    for n in range(9, 12):
                        proj(at, n)
                    fill = {}
                    for u in range(UNITS):
                        fill[u, 0] = [(unit_1, u)]
                        fill[u, 1] = [(unit_2, u)]
                        fill[u, 2] = [(unit_3, u)]
                    for i in range(NB - 1):
                        fill[2 * i + 2, 2].append((ho_T, i))
                    fill[8, 1] = [(ho_T, NB - 1)]
                    fill[8, 2] = [(out_proj, 0)]
                    fill[9, 0] = [(out_proj, 1)]
                    fill[9, 1] = [(out_proj, 2)]
                    fill[9, 2] = [(out_proj, 3)]
                    fill[10, 0] = [(h2_T, 0), (h2_T, 1)]
                    fill[10, 1] = [(h2_T, 2), (h2_T, 3)]
                    for t in range(NF):
                        gate(at, t, slot(t), XT)
                        for f, a in fill.get((t, 0), []):
                            f(at, a)
                        up(at, t, slot(t), XT)
                        for f, a in fill.get((t, 1), []):
                            f(at, a)
                        if t:
                            if t == 1:
                                pe.wait_ge(vec_out.sem, vec_out.before(at))
                            down(at, t - 1, slot(t - 1), first=t == 1)
                        for f, a in fill.get((t, 2), []):
                            f(at, a)
                    wait(pe, vec_h2T, at, NB - 1, "lo")
                    pe.sem_inc(pe_passed, 1)
                    with pe.Fori(0, LOOPED // 2) as i:
                        for q in range(2):
                            t = i * 2 + (NF + q)
                            gate(at, t, slot(NF + q), HT)
                            up(at, t, slot(NF + q), HT)
                            down(at, t + -1, slot(NF + q - 1))
                    for t in range(NF + LOOPED, NT):
                        gate(at, t, slot(t), HT)
                        if NT - 3 <= t < NT - 1:
                            x_T(at, t - NT + 3, XN[1 - half])
                        up(at, t, slot(t), HT)
                        down(at, t - 1, slot(t - 1))
                    x_T(at, 2, XN[1 - half])
                    x_T(at, 3, XN[1 - half])
                    down(at, NT - 1, slot(NT - 1), last=True)

        @block.scalar
        def _(act):
            def x_T(at, i):
                wait(act, pe_xT, at, i)
                act.activation(XT[0][:, :, i * P:(i + 1) * P], AB[i % 2][:].rearrange("p (k n) -> p k n", k=KT),
                               ACT.Copy).then_inc(act_xT.sem, 1)

            def w_gu(at, k, slot, n_loads):
                act.wait_ge(ld_gu[slot], n_loads)
                act.wait_ge(pe_up.sem, pe_up.of(at, k, "done") - 2)
                act.activation(WGU[0][:, slot, :], raw_gu[:, slot, :], ACT.Copy).then_inc(act_wgu.sem, 1)

            def w_dn(at, k, slot):
                act.wait_ge(ld_dn, load_count_dn(at, k))
                act.wait_ge(pe_down.sem, pe_down.of(at, k, "done") - 2)
                act.activation(WDN[0][:, slot, :], raw_dn[:], ACT.Copy).then_inc(act_wdn.sem, 1)

            def load_count_dn(at, k):
                return at[0] * (HALVES * NT * 16) + k * 16 + (at[1] * NT * 16 + 16)

            def gu_loads(at, j):
                b, half = at
                return b * (NT * 16) + ((half * NT + j) // 2 + 1) * 16

            def tanh(at, t):
                wait(act, pe_gate, at, t)
                if isinstance(t, int) and t == 0:
                    wait(act, vec_o, at, NB - 1)
                act.wait_ge(vec_hm.sem, vec_hm.of(at, t, "done") - 1)
                act.activation(th[:], GB[:], ACT.Tanh, scale=0.5).then_inc(act_tanh.sem, 1)

            def hid(at, t):
                wait(act, vec_hm, at, t)
                act.wait_ge(pe_down.sem, pe_down.of(at, t, "done") - 1)
                act.activation(HH[0][:], hm[:], ACT.Copy).then_inc(act_hid.sem, 1)

            act.sem_inc(look_act, 1)

            def upper_weights(pieces):
                for m in pieces:
                    act.wait_ge(vec_pre, m + 1)
                    hi, raw = (WG[0][:, :, :], raw_w[0][:, 0:KT * 2 * H]) if m == 8 else \
                        (WA[0][:, m // 2, (m % 2) * 2:(m % 2) * 2 + 2, :], raw_w[m % 4])
                    act.activation(hi.rearrange("p k n -> p (k n)"), raw, ACT.Copy).then_inc(act_pre, 1)

            upper_weights(range(4))
            for i in range(NB):
                x_T(PRE, i)
            upper_weights(range(4, 9))
            act.wait_ge(vec_const, 7)
            def look_up(t, first=False):
                for c in range(3):
                    act.wait_ge(look_vec, t * LOOK_V + ((c - 1) * LOOK_C + LOOK_CREDIT + 4))
                    if not first:
                        act.wait_ge(st_w[c], t * 16)
                    for k in range(LUT // 2):
                        if k:
                            act.wait_ge(look_vec, t * LOOK_V + ((c - 1) * LOOK_C + LOOK_CREDIT + LOOK_FREES[k]))
                        act.activation(wbuf[c] if k == 0 else BANKS[k][:], b0[c].bitcast(i32), ACT.Identity,
                                       bias=lt[:, 2 * k:2 * k + 1], scale=ld[:, k:k + 1]).then_inc(look_act, 1)

            look_up(0, first=True)
            with act.Fori(1, NF) as t:
                look_up(t)
            w_gu((0, 0), 0, 0, 16)
            with act.Fori(0, BATCH) as b:
                for half in range(HALVES):
                    at = (b, half)
                    before = (b, half - 1)
                    R1 = r1[half]
                    g_, sp_, a_, rw = rows(half)

                    def logits():
                        wait(act, pe_gates, at, 0, "logits")
                        act.activation(gts[:, :], UB[0:2 * H, :], ACT.Copy).then_inc(act_gates.sem, 1)

                    def qk(i):
                        wait(act, pe_qk, at, i)
                        if i >= 2:
                            wait(act, pe_qkT, at, i - 2)
                        else:
                            act.wait_ge(pe_unit.sem, pe_unit.before(at))
                        act.activation(qn[:, i % 2, :], AB[i % 2][:, 0:H * DQ], ACT.Copy, scale=R1[:, 1, i:i + 1])\
                            .then_inc(act_qk.sem, 1)
                        act.activation(kn[:, i, :], AB[i % 2][:, H * DQ:], ACT.Copy, scale=R1[:, 0, i:i + 1])\
                            .then_inc(act_qk.sem, 1)

                    def qkT_(i):
                        wait(act, pe_qkT, at, i)
                        if i == 0:
                            act.wait_ge(vec_res.sem, vec_res.before(at))
                        for z in range(2):
                            act.activation(qkT[:, z, :, i * P:(i + 1) * P],
                                           GB[:, z * G * P:(z + 1) * G * P].rearrange("p (g n) -> p g n", g=G),
                                           ACT.Copy).then_inc(act_qkT.sem, 1)

                    def v(i):
                        wait(act, pe_v, at, i)
                        act.activation(va[:, i * H * VS:(i + 1) * H * VS].rearrange("p (h d) -> p h d", h=H)[:, :, 0:DV],
                                       AB[i % 2][:].rearrange("p (h d) -> p h d", h=H), ACT.Copy,
                                       scale=R1[:, 0, i:i + 1]).then_inc(act_v.sem, 1)

                    def o(i):
                        wait(act, pe_o, at, i)
                        if i < 2:
                            act.wait_ge(pool_hid.sem, pool_hid.before(at))
                        else:
                            wait(act, vec_o, at, i - 2)
                        act.activation(to[i % 2][:], AB[i % 2][:], ACT.Tanh, scale=R1[:, 2, i:i + 1])\
                            .then_inc(act_o.sem, 1)

                    logits()
                    qk(0)
                    qk(1)
                    qkT_(0)
                    wait(act, vec_rows, at, 0, "biased")
                    act.activation(gt[:, :, 0:H], gn2[:, :, 0:H], ACT.Tanh, scale=1 / CAP).then_inc(act_gates.sem, 1)
                    act.activation(tf[:, :, :], gn2[:, :, H:], ACT.Tanh, scale=1 / CAP).then_inc(act_gates.sem, 1)
                    wait(act, act_gates, at, 0, "tanh_f")
                    act.activation(ef[:, :, :], tf[:, :, :], ACT.Exp, scale=-CAP).then_inc(act_gates.sem, 1)
                    wait(act, act_gates, at, 0, "exp")
                    act.activation(gt[:, :, 32:40], ef[:, :, :], ACT.Ln, bias=1.0).then_inc(act_gates.sem, 1)
                    qk(2)
                    qkT_(1)
                    qk(3)
                    wait(act, pe_gates, at, 0, "rows")
                    act.activation(sp_, UB[32:40, :], ACT.Copy).then_inc(act_gates.sem, 1)
                    qkT_(2)
                    v(0)
                    qkT_(3)
                    wait(act, vec_rows, at, 0, "a_hi")
                    act.activation(AL[64:64 + H, :], ah.bitcast(f32), ACT.Copy).then_inc(act_gates.sem, 1)
                    v(1)
                    v(2)
                    wait(act, vec_rows, at, 0, "bound")
                    for r in range(0, RW, 32):
                        act.activation(rwe[r:r + H, :], rw[r:r + H, :], ACT.Exp).then_inc(act_gates.sem, 1)
                    v(3)
                    def qbd_(u):
                        j, g = u // G, u % G
                        if u:
                            wait(act, pe_unit, at, u - 1, "scores")
                        else:
                            wait(act, vec_h2T, before, NB - 1, "lo")
                        wait(act, act_qkT, at, j, "q")
                        for h in range(HG):
                            act.activation(qbd[:, h, :], qkT[:, 0, g, j * P:(j + 1) * P], ACT.Copy,
                                           scale=bdm[:, h:h + 1]).then_inc(act_qbd.sem, 1)

                    for i in range(NB):
                        o(i)
                    qbd_(0)

                    def unit(u):
                        wait(act, vec_unit, at, u, "masked")
                        if u == 0:
                            wait(act, pe_gates, at, 0, "factors")
                        act.activation(ex[:, :, :], ar[:, :, :], ACT.Exp).then_inc(act_unit.sem, 1)

                    def ho_T(i):
                        wait(act, pe_hoT, at, i)
                        act.activation(HT[0][:, :, i * P:(i + 1) * P], A[:].rearrange("p (k n) -> p k n", k=KT),
                                       ACT.Copy).then_inc(act_hoT.sem, 1)

                    def h2_T(i):
                        wait(act, vec_h2S, at, i, "scaled")
                        wait(act, pe_out, at, i)
                        act.activation(HT[0][:, :, i * P:(i + 1) * P], ct[:, :, :] if i % 2 else qbd[:, :, :],
                                       ACT.Copy).then_inc(act_h2T.sem, 1)

                    for t in range(NF):
                        slot = (half * NT + t) % 2
                        if t:
                            hid(at, t - 1)
                        w_gu(at, t + 1, 1 - slot, gu_loads(at, t + 1))
                        tanh(at, t)
                        if t < UNITS:
                            unit(t)
                        if t == 10:
                            for i in range(NB):
                                h2_T(i)
                        w_dn(at, t, slot)
                        if t + 1 < UNITS:
                            qbd_(t + 1)
                        if t in (2, 4, 6):
                            ho_T(t // 2 - 1)
                        if t == 8:
                            ho_T(NB - 1)
                    with act.Fori(0, LOOPED // 2) as i:
                        for q in range(2):
                            t = i * 2 + (NF + q)
                            slot = (half * NT + NF + q) % 2
                            hid(at, t + -1)
                            w_gu(at, t + 1, 1 - slot, i * 16 + gu_loads(at, NF + q + 1))
                            tanh(at, t)
                            w_dn(at, t, slot)
                    for t in range(NF + LOOPED, NT):
                        slot = (half * NT + t) % 2
                        hid(at, t - 1)
                        w_gu(at, t + 1, 1 - slot, gu_loads(at, t + 1))
                        tanh(at, t)
                        w_dn(at, t, slot)
                        if NT - 3 <= t < NT - 1:
                            x_T(at, t - NT + 3)
                    hid(at, NT - 1)
                    x_T(at, 2)
                    x_T(at, 3)
                    for i in range(NB):
                        wait(act, vec_out, at, i)
                        act.dma_start(out[bass.ds((b * HALVES + half) * TOK + i * P, P), :], XN[half][:, i, :])\
                            .then_inc(st_out[half], 16)
            for s in st_out:
                act.wait_ge(s, 16 * NB * BATCH)

        @block.vector
        def _(dve):
            for s in (vec_hm, vec_out, vec_res, vec_gate, vec_h2T):
                dve.sem_inc(s.sem, s.credit)
            def ln_stats(at, xs, par, loads):
                dve.wait_ge(ld_x[par], loads)
                for i in range(NB):
                    dve.bn_stats(st6[:, i, :], xs[:, i, :]).then_inc(vec_ln.sem, 1)
                wait(dve, vec_ln, at, 0, f"stats{NB - 1}")
                dve.sem_inc(vec_passed, 1)
                for i in range(NB):
                    dve.bn_aggr(mv[:, i, :], st6[:, i, :]).then_inc(vec_ln.sem, 1)
                wait(dve, vec_ln, at, 0, f"mv{NB - 1}")
                dve.tensor_scalar(ve[:], mv[:, :, 1], EPS_LN, None, ALU.add).then_inc(vec_ln.sem, 1)

            def ln_square(at):
                wait(dve, pool_ln, at, 0, "root")
                dve.tensor_tensor(ve[:], rs[:], rs[:], ALU.mult).then_inc(vec_ln.sem, 1)
                wait(dve, vec_ln, at, 0, "r2")
                dve.tensor_tensor(ve[:], ve[:], mv[:, :, 1], ALU.mult).then_inc(vec_ln.sem, 1)
                wait(dve, vec_ln, at, 0, "vr")
                dve.tensor_scalar(ve[:], ve[:], EPS_RMS, None, ALU.add).then_inc(vec_ln.sem, 1)

            def ln_apply(at, xs, par):
                wait(dve, pool_ln, at, 0, "root1")
                dve.tensor_scalar(r1[par][:, 1, :], r1[par][:, 0, :], QSCALE, None, ALU.mult).then_inc(vec_ln.sem, 1)
                dve.tensor_scalar(r1[par][:, 2, :], r1[par][:, 0, :], 0.5, None, ALU.mult).then_inc(vec_ln.sem, 1)
                for i in range(NB):
                    dve.tensor_scalar(xs[:, i, :], xs[:, i, :], mv[:, i, 0:1], rs[:, i:i + 1], ALU.subtract, ALU.mult)\
                        .then_inc(vec_ln.sem, 1)

            def scale_weights(pieces):
                for m in pieces:
                    dve.wait_ge(ld_w[m % 4], 16 * (m // 4 + 1))
                    ks = range(KT) if m == 8 else range((m % 2) * 2, (m % 2) * 2 + 2)
                    n = 2 * H if m == 8 else D
                    for z, k in enumerate(ks):
                        w = raw_w[m % 4][:, z * n:(z + 1) * n]
                        last = dve.tensor_scalar(w, w, 1.0 if m in (6, 7) else n1[:, k:k + 1], None, ALU.mult)
                    last.then_inc(vec_pre, 1)

            ln_stats(PRE, XN[0], 0, 16)
            ln_square(PRE)
            ln_apply(PRE, XN[0], 0)
            dve.wait_ge(ld_const, 16 * 5)
            scale_weights(range(4))
            dve.wait_ge(pool_const, POOL_CONSTS)
            dve.wait_ge(ld_const, 16 * 5)
            n = 0

            def const(ins):
                nonlocal n
                n += 1
                ins.then_inc(vec_const, 1)

            const(dve.tensor_reduce(bdm[:], ident[:].rearrange("p (h d) -> p h d", h=HG), AX.X, ALU.add))
            const(dve.tensor_reduce(hm32[:], ident[:].rearrange("p (a d) -> p d a", d=32), AX.X, ALU.add))
            const(dve.tensor_copy(rep[:, :, :], ident[0:H, 0:H].unsqueeze(2).to_broadcast([H, H, DQ])))
            const(dve.tensor_copy(MX[64:64 + H, :, :], ident[64:64 + H, 64:64 + H].unsqueeze(2).to_broadcast([H, H, P])))
            const(dve.tensor_copy(MX[96:96 + H, :, :], ident[96:96 + H, 96:96 + H].unsqueeze(2).to_broadcast([H, H, P])))
            const(dve.tensor_scalar(mhb[:], mhb[:], 0.5, None, ALU.mult))
            const(dve.tensor_tensor(ld[:], lt[:, 1::2], lt[:, 0::2], ALU.subtract))

            def x_T(at, i):
                wait(dve, act_xT, at, i, "hi")
                dve.tensor_tensor(XT[1][:, :, i * P:(i + 1) * P], AB[i % 2][:].rearrange("p (k n) -> p k n", k=KT),
                                  XT[0][:, :, i * P:(i + 1) * P].bitcast(f32), ALU.subtract).then_inc(vec_xT.sem, 1)

            for i in range(NB):
                x_T(PRE, i)
            scale_weights(range(4, 9))
            def bit(dst, src, n):
                dve.tensor_scalar(dst.bitcast(i32), src, 1 << n, None, ALU.bitwise_and).then_inc(look_vec, 1)

            first = LOOK_CREDIT - LOOK_C + 4
            dve.sem_inc(look_vec, first - 1)
            dve.wait_ge(ld_idx[0], 16)
            bit(b0[0], ixb[0], 0)
            dve.wait_ge(look_vec, first)
            dve.sem_inc(look_vec, LOOK_CREDIT - first)
            with dve.Fori(0, NF) as t:
                for c in range(3):
                    at_v = t * LOOK_V + (c * LOOK_C + LOOK_CREDIT)
                    at_a = t * (3 * LUT // 2) + (c * (LUT // 2) + 1)
                    dve.wait_ge(ld_idx[c], t * 16 + 16)
                    dve.wait_ge(look_vec, at_v)
                    for n, dst in enumerate(bits):
                        bit(dst, ixb[c], n + 1)
                    after = (c + 1) % 3
                    dve.wait_ge(ld_idx[after], t * 16 + (16 if after else 32))
                    dve.wait_ge(look_act, at_a)
                    bit(b0[after], ixb[after], 0)
                    dve.wait_ge(look_vec, at_v + 4)
                    for n, (lower, bit_n, upper, level) in enumerate(MUX):
                        dve.wait_ge(look_act, at_a + (max(lower, upper) + 1 if level == 1 else 0))
                        if LOOK_NEEDS[n]:
                            dve.wait_ge(look_vec, at_v + (4 + LOOK_NEEDS[n]))
                        dve.sem_inc(vec_passed, 1)
                        dve.copy_predicated(wbuf[c] if lower == 0 else BANKS[lower][:], bits[bit_n].bitcast(i32),
                                            BANKS[upper][:]).then_inc(look_vec, 1)
            last_row = INTER - (NF - 1) * P
            dve.memset(zero_rows[last_row:P, :], 0.0).then_inc(vec_pre, 1)

            def gated(at, t):
                wait(dve, act_tanh, at, t)
                dve.scalar_tensor_tensor(th[:], th[:], 1.0, GB[:], ALU.add, ALU.mult).then_inc(vec_gate.sem, 1)

            def product(at, t):
                wait(dve, pe_up, at, t)
                wait(dve, vec_gate, at, t)
                dve.wait_ge(pool_hid.sem, pool_hid.of(at, t, "lo") - 1)
                dve.scalar_tensor_tensor(hm[:], th[:], 0.5, UB[:], ALU.mult, ALU.mult).then_inc(vec_hm.sem, 1)

            with dve.Fori(0, BATCH) as b:
                for half in range(HALVES):
                    at = (b, half)
                    before = (b, half - 1)
                    R1 = r1[half]
                    g_, sp_, a_, rw = rows(half)
                    OG = og(half)

                    def row(name):
                        assert ROWS[row.n] == name
                        row.n += 1
                        return lambda ins: ins.then_inc(vec_rows.sem, 1)
                    row.n = 0

                    if half:
                        dve.wait_ge(st_out[0], b * (16 * NB) + 16 * NB)
                    else:
                        dve.wait_ge(out_left, b + 1)
                    wait(dve, pe_gates, at, 0, "natural")
                    row("scaled")(dve.tensor_tensor(
                        gn[:, :, :], UB[:, 0:NB * 2 * H].rearrange("p (i n) -> p i n", i=NB),
                        R1[:, 0, :].unsqueeze(2).to_broadcast([P, NB, 2 * H]), ALU.mult))
                    wait(dve, vec_rows, at, 0, "scaled")
                    row("biased")(dve.tensor_tensor(gn2[:, :, :], gn[:, :, :],
                                                    gb[:].unsqueeze(1).to_broadcast([P, NB, 2 * H]), ALU.add))
                    if half:
                        row("m0")(dve.tensor_copy(mx[:, 0:1], mx[:, TOK:TOK + 1]))
                        row("g0")(dve.tensor_copy(gcar[:], gcar[:]))
                    else:
                        row("m0")(dve.memset(mx[:, 0:1], FAR))
                        row("g0")(dve.memset(gcar[:], 0.0))
                    wait(dve, vec_rows, at, 0, "g0")
                    wait(dve, act_gates, at, 0, "f_rows")
                    row("cum")(dve.tensor_tensor_scan(g_, one[:].to_broadcast([H, TOK]), sp_, gcar[:], ALU.mult, ALU.add))
                    wait(dve, vec_rows, at, 0, "cum")
                    row("a")(dve.scalar_tensor_tensor(a_, UB[0:H, :], CAP, g_, ALU.mult, ALU.add))
                    wait(dve, vec_rows, at, 0, "a")
                    row("a_hi")(dve.tensor_copy(ah, a_))
                    wait(dve, vec_rows, at, 0, "a_hi")
                    row("a_lo")(dve.tensor_tensor(AL[96:96 + H, :], a_, ah.bitcast(f32), ALU.subtract))
                    row("max")(dve.tensor_tensor_scan(mx[:, 1:], a_, a_, mx[:, 0:1], ALU.max, ALU.max))
                    wait(dve, vec_rows, at, 0, "max")
                    dve.wait_ge(pool_mx.sem, pool_mx.before(at))
                    row("m_hi")(dve.tensor_scalar(mhl[0:H, :].bitcast(f32r), mx[:, 1:], -1.0, None, ALU.mult))
                    wait(dve, vec_rows, at, 0, "m_hi")
                    row("m_lo")(dve.scalar_tensor_tensor(mhl[32:32 + H, :], mx[:, 1:], -1.0, mhl[0:H, :],
                                                         ALU.mult, ALU.subtract))
                    blocks = "p (j n) -> p j n"
                    start = mx[:, 0:TOK:P].unsqueeze(2).to_broadcast([H, NB, P])
                    end = mx[:, P:TOK + 1:P].unsqueeze(2).to_broadcast([H, NB, P])
                    row("inter")(dve.tensor_tensor(rw[0:H, :].rearrange(blocks, j=NB), start,
                                                   mx[:, 1:].rearrange(blocks, j=NB), ALU.subtract))
                    row("keys")(dve.tensor_tensor(rw[32:32 + H, :].rearrange(blocks, j=NB),
                                                  a_.rearrange(blocks, j=NB), end, ALU.subtract))
                    row("bound")(dve.tensor_tensor(rw[64:64 + H, :], g_, mx[:, 1:], ALU.subtract))
                    row("carry")(dve.tensor_copy(gcar[:], g_[:, TOK - 1:TOK]))
                    wait(dve, pe_gates, at, 0, "factors")
                    row("factors")(dve.tensor_copy(rn[:], UB[:, 0:NB * RW + G * NB]))
                    for i in range(NB):
                        wait(dve, act_o, at, i)
                        if i == 0:
                            wait(dve, act_gates, at, 0, "exps")
                            wait(dve, vec_rows, at, 0, "factors")
                        dve.scalar_tensor_tensor(OG[:, i, :], to[i % 2][:], 1.0, mhb[:], ALU.add, ALU.mult)\
                            .then_inc(vec_o.sem, 1)

                    def factor(j, kind, h0, hs, width):
                        c = j * RW + kind * 32 + h0
                        return rn[:, c:c + hs].unsqueeze(2).to_broadcast([P, hs, width])

                    def unit_1(u):
                        wait(dve, pe_unit, at, u, "exponents")
                        if u:
                            wait(dve, act_unit, at, u - 1, "exp")
                        if u == 0:
                            wait(dve, pe_gates, at, 0, "natural")
                        if u and u % 2 == 0:
                            wait(dve, vec_norm, at, u // 2 - 1, "sums")
                        dve.tensor_tensor(ar[:, :, :], A[:].rearrange("p (h n) -> p h n", h=HG),
                                          maskd[:].unsqueeze(1).to_broadcast([P, HG, P]), ALU.min)\
                            .then_inc(vec_unit.sem, 1)

                    def weights(u):
                        wait(dve, act_unit, at, u, "exp")
                        wait(dve, pe_unit, at, u, "scores")
                        dve.tensor_tensor(ct[:, :, :], B[:].rearrange("p (h n) -> p h n", h=HG), ex[:, :, :], ALU.mult)\
                            .then_inc(vec_unit.sem, 1)

                    def unit_2(u):
                        j, g = u // G, u % G
                        wait(dve, pe_unit, at, u, "values")
                        if u:
                            wait(dve, vec_unit, at, u - 1, "state")
                        dve.tensor_tensor(tt[:, :, :], B[:, 0:HG * VS].rearrange("p (h n) -> p h n", h=HG),
                                          factor(j, 0, g * HG, HG, VS), ALU.mult).then_inc(vec_unit.sem, 1)
                        wait(dve, vec_unit, at, u, "before")
                        dve.tensor_tensor(hr[:, g * HG:(g + 1) * HG, :],
                                          A[:].rearrange("p (h n) -> p h n", h=HG)[:, :, 0:VS], tt[:, :, :], ALU.add)\
                            .then_inc(vec_unit.sem, 1)

                    def unit_3(u):
                        j, g = u // G, u % G
                        wait(dve, pe_unit, at, u, "state")
                        wait(dve, vec_unit, at, u, "heads")
                        dve.tensor_tensor(tt[:, :, :], B[:, 0:HG * VS].rearrange("p (h n) -> p h n", h=HG),
                                          bdm[:].unsqueeze(2).to_broadcast([P, HG, VS]), ALU.mult)\
                            .then_inc(vec_unit.sem, 1)
                        wait(dve, vec_unit, at, u, "update")
                        c = NB * RW + g * NB + j
                        dve.scalar_tensor_tensor(kv[:, g, :, :], kv[:, g, :, :], rn[:, c:c + 1], tt[:, :, :],
                                                 ALU.mult, ALU.add).then_inc(vec_unit.sem, 1)

                    def norm_1(j):
                        c = j * RW + 64
                        wait(dve, vec_unit, at, 2 * j + 1, "heads")
                        dve.scalar_tensor_tensor(nm[:], hr[:, :, DV], -1.0, hr[:, :, DV], ALU.mult, ALU.max)\
                            .then_inc(vec_norm.sem, 1)
                        wait(dve, vec_norm, at, j, "size")
                        dve.tensor_tensor(nm[:], nm[:], rn[:, c:c + H], ALU.max).then_inc(vec_norm.sem, 1)
                        wait(dve, vec_norm, at, j, "floor")
                        dve.reciprocal(sm[:], nm[:]).then_inc(vec_norm.sem, 1)
                        wait(dve, vec_norm, at, j, "inverse")
                        if j:
                            wait(dve, pe_hoT, at, j - 1)
                        dve.tensor_tensor(hn[:, :, :], hr[:, :, 0:DV], sm[:].unsqueeze(2).to_broadcast([P, H, DV]),
                                          ALU.mult).then_inc(vec_norm.sem, 1)
                        wait(dve, vec_norm, at, j, "divided")
                        wait(dve, act_unit, at, 2 * j + 1, "exp")
                        dve.tensor_tensor(sq[:, :, :], hn[:, :, :], hn[:, :, :], ALU.mult).then_inc(vec_norm.sem, 1)
                        wait(dve, vec_norm, at, j, "squares")
                        dve.tensor_reduce(nm[:], sq[:, :, :], AX.X, ALU.add).then_inc(vec_norm.sem, 1)
                        wait(dve, vec_norm, at, j, "sums")
                        dve.tensor_scalar(sm[:], nm[:], 1 / DV, EPS_RMS, ALU.mult, ALU.add).then_inc(vec_norm.sem, 1)

                    def norm_2(j):
                        wait(dve, pool_norm, at, j, "root")
                        dve.tensor_tensor(hn[:, :, :], hn[:, :, :], rh[:].unsqueeze(2).to_broadcast([P, H, DV]),
                                          ALU.mult).then_inc(vec_norm.sem, 1)
                        wait(dve, vec_norm, at, j, "scaled")
                        wait(dve, vec_o, at, NB - 1)
                        dve.tensor_tensor(hn[:, :, :], hn[:, :, :], OG[:, j, :].rearrange("p (h d) -> p h d", h=H),
                                          ALU.mult).then_inc(vec_norm.sem, 1)

                    def ho_T(j):
                        wait(dve, act_hoT, at, j, "hi")
                        dve.tensor_tensor(HT[1][:, :, j * P:(j + 1) * P], A[:].rearrange("p (k n) -> p k n", k=KT),
                                          HT[0][:, :, j * P:(j + 1) * P].bitcast(f32), ALU.subtract)\
                            .then_inc(vec_hoT.sem, 1)

                    def x1_(i):
                        wait(dve, pe_out, at, i)
                        dve.tensor_tensor(XN[half][:, i, :], XN[half][:, i, :], AB[i % 2][:], ALU.add)\
                            .then_inc(vec_x1.sem, 1)
                        wait(dve, vec_x1, at, i, "x1")
                        dve.bn_stats(st6[:, i, :], XN[half][:, i, :]).then_inc(vec_x1.sem, 1)
                        wait(dve, vec_x1, at, i, "stats")
                        dve.sem_inc(vec_passed, 1)
                        dve.bn_aggr(mv[:, i, :], st6[:, i, :]).then_inc(vec_x1.sem, 1)
                        wait(dve, vec_x1, at, i, "mv")
                        dve.scalar_tensor_tensor(ve[:, i:i + 1], mv[:, i, 0:1], mv[:, i, 0:1], mv[:, i, 1:2],
                                                 ALU.mult, ALU.add).then_inc(vec_x1.sem, 1)
                        wait(dve, vec_x1, at, i, "ms")
                        dve.tensor_scalar(ve[:, i:i + 1], ve[:, i:i + 1], EPS_RMS, None, ALU.add).then_inc(vec_x1.sem, 1)

                    def h2_(i):
                        wait(dve, pool_x1, at, i, "root")
                        if i == 3:
                            wait(dve, pe_h2T, at, 0)
                        dve.tensor_scalar(h2_rows[i], XN[half][:, i, :], rs[:, i:i + 1], None, ALU.mult)\
                            .then_inc(vec_h2.sem, 1)

                    def h2_scale(i):
                        wait(dve, pe_h2T, at, i)
                        if i >= 2:
                            wait(dve, act_h2T, at, i - 2, "hi")
                            wait(dve, vec_h2T, at, i - 2, "lo")
                        dst = ct if i % 2 else qbd
                        dve.tensor_tensor(dst[:, :, :], AB[i % 2][:].rearrange("p (k n) -> p k n", k=KT),
                                          n2[:].unsqueeze(2).to_broadcast([P, KT, P]), ALU.mult)\
                            .then_inc(vec_h2S.sem, 1)

                    def h2_lo(i):
                        dst = ct if i % 2 else qbd
                        wait(dve, act_h2T, at, i, "hi")
                        dve.tensor_tensor(HT[1][:, :, i * P:(i + 1) * P], dst[:, :, :],
                                          HT[0][:, :, i * P:(i + 1) * P].bitcast(f32), ALU.subtract)\
                            .then_inc(vec_h2T.sem, 1)

                    if half == 0:
                        dve.wait_ge(pe_unit.sem, pe_unit.before(at))
                        dve.memset(kv[:, :, :, :], 0.0).then_inc(vec_const, 1)
                        dve.wait_ge(vec_const, b * 1 + (8))
                    for t in range(NF):
                        if t == 8:
                            norm_2(NB - 1)
                        if t == 9:
                            x1_(0)
                        if t < UNITS:
                            unit_1(t)
                        gated(at, t)
                        if t < UNITS:
                            weights(t)
                        if t == 9:
                            x1_(1)
                        if t == 10:
                            h2_(2)
                            h2_scale(0)
                            h2_(3)
                            h2_scale(1)
                            h2_lo(0)
                            h2_scale(2)
                            h2_lo(1)
                            h2_scale(3)
                            h2_lo(2)
                            h2_lo(3)
                        product(at, t)
                        if t < UNITS:
                            if t in (2, 4, 6):
                                norm_2(t // 2 - 1)
                            unit_2(t)
                            if t == UNITS - 1:
                                norm_1(NB - 1)
                            unit_3(t)
                            if t in (2, 4, 6):
                                ho_T(t // 2 - 1)
                            if t % 2 and t < UNITS - 1:
                                norm_1(t // 2)
                        if t == 8:
                            ho_T(NB - 1)
                        if t == 9:
                            h2_(0)
                            x1_(2)
                            x1_(3)
                            h2_(1)
                    with dve.Fori(0, LOOPED // 2) as i:
                        for q in range(2):
                            t = i * 2 + (NF + q)
                            gated(at, t)
                            product(at, t)
                    for t in range(NF + LOOPED, NT):
                        gated(at, t)
                        product(at, t)
                        if t == NF + LOOPED:
                            dve.wait_ge(ld_xr, b * (16 * HALVES) + (half + 1) * 16)
                            for i in range(NB):
                                dve.tensor_tensor(XN[half][:, i, :], XN[half][:, i, :], xr[:, i, :], ALU.add)\
                                    .then_inc(vec_res.sem, 1)
                            ln_stats(at, XN[1 - half], 1 - half, b * 16 + (16 + 16 * half))
                        if t == NF + LOOPED + 1:
                            ln_square(at)
                        if t == NF + LOOPED + 2:
                            ln_apply(at, XN[1 - half], 1 - half)
                        if NT - 3 <= t < NT - 1:
                            x_T(at, t - NT + 3)
                    x_T(at, 2)
                    x_T(at, 3)
                    wait(dve, pe_down, at, NT - 1)
                    wait(dve, vec_res, at, NB - 1)
                    for i in range(NB):
                        dve.tensor_tensor(XN[half][:, i, :], XN[half][:, i, :], ACC[i][:], ALU.add)\
                            .then_inc(vec_out.sem, 1)

        @block.gpsimd
        def _(pool):
            done = 0

            def const(ins):
                nonlocal done
                done += 1
                ins.then_inc(pool_const, 1)
                pool.wait_ge(pool_const, done)

            const(pool.memset(half_pow[:], -0.5))
            const(pool.memset(ident[:], 0.0))
            const(pool.memset(maskd[:], 0.0))
            const(pool.memset(AL[:, :].bitcast(i32), 0))
            def root(dst, src, n, stage):
                pool.tensor_tensor(dst, src, half_pow[:, 0:n], ALU.pow).then_inc(stage.sem, 1)

            def ln_root(at):
                wait(pool, vec_ln, at, 0, "ve")
                root(rs[:], ve[:], NB, pool_ln)

            def ln_root1(at, par):
                wait(pool, vec_ln, at, 0, "ve1")
                root(r1[par][:, 0, :], ve[:], NB, pool_ln)

            ln_root(PRE)
            ln_root1(PRE, 0)
            const(pool.affine_select(out=ident[:], in_=ident[:], compare_op=ALU.not_equal, fill=1.0, base=0,
                                     pattern=[[-1, P]], channel_multiplier=1))
            const(pool.affine_select(out=maskd[:], in_=maskd[:], compare_op=ALU.is_ge, fill=MASKED, base=0,
                                     pattern=[[1, P]], channel_multiplier=-1))
            const(pool.memset(AL[0:H, :].bitcast(f32), 1.0))
            const(pool.memset(AL[32:32 + H, :].bitcast(f32), 1.0))
            const(pool.memset(MX[:, :, :].bitcast(i32), 0))
            const(pool.memset(va[:], 1.0))
            const(pool.memset(mhl[:], 0.0))
            const(pool.memset(gt[:, :, :], 0.0))
            const(pool.memset(one[:], 1.0))
            assert done == POOL_CONSTS

            for s in (pool_mx, pool_hid):
                pool.sem_inc(s.sem, s.credit)
            pool.sem_inc(pool_wgu.sem, 2)
            pool.sem_inc(pool_wdn.sem, 1)
            for m in range(9):
                pool.wait_ge(act_pre, m + 1)
                k = (m % 2) * 2
                lo, hi, raw = (WG[1][:, :, :], WG[0][:, :, :], raw_w[0][:, 0:KT * 2 * H]) if m == 8 else \
                    (WA[1][:, m // 2, k:k + 2, :], WA[0][:, m // 2, k:k + 2, :], raw_w[m % 4])
                pool.tensor_tensor(lo.rearrange("p k n -> p (k n)"), raw, hi.rearrange("p k n -> p (k n)").bitcast(f32),
                                   ALU.subtract).then_inc(pool_pre, 1)
            with pool.Fori(0, NF) as t:
                for c in range(3):
                    pool.wait_ge(look_vec, t * LOOK_V + ((c + 1) * LOOK_C + LOOK_CREDIT))
                    pool.dma_start(ffn[bass.ds(t, 1), :, c * D:(c + 1) * D].rearrange("a p n -> (a p) n"), wbuf[c])\
                        .then_inc(st_w[c], 16)
            pool.wait_ge(vec_pre, 10)
            pool.wait_ge(st_w[2], 16 * NF)
            first = INTER - (NF - 1) * P
            pool.dma_start(ffn[NF - 1, first:P, GU:], zero_rows[first:P, :]).then_inc(st_zero, 16)

            def w_gu(at, k, slot):
                wait(pool, act_wgu, at, k, "hi")
                pool.tensor_tensor(WGU[1][:, slot, :], raw_gu[:, slot, :], WGU[0][:, slot, :].bitcast(f32), ALU.subtract)\
                    .then_inc(pool_wgu.sem, 1)

            def w_dn(at, k, slot):
                wait(pool, act_wdn, at, k, "hi")
                pool.tensor_tensor(WDN[1][:, slot, :], raw_dn[:], WDN[0][:, slot, :].bitcast(f32), ALU.subtract)\
                    .then_inc(pool_wdn.sem, 1)

            def hid(at, t):
                wait(pool, act_hid, at, t, "hi")
                pool.tensor_tensor(HH[1][:], hm[:], HH[0][:].bitcast(f32), ALU.subtract).then_inc(pool_hid.sem, 1)

            w_gu((0, 0), 0, 0)
            with pool.Fori(0, BATCH) as b:
                for half in range(HALVES):
                    at = (b, half)
                    before = (b, half - 1)

                    def mx_(j):
                        if j:
                            wait(pool, pe_unit, at, 2 * j - 1, "exponents")
                        else:
                            wait(pool, vec_rows, at, 0, "m_lo")
                        n = 32 + H
                        pool.tensor_tensor(MX[0:n, :, :], mhl[0:n, j * P:(j + 1) * P].unsqueeze(1).to_broadcast([n, H, P]),
                                           hm32[0:n, 0:H].unsqueeze(2).to_broadcast([n, H, P]), ALU.mult)\
                            .then_inc(pool_mx.sem, 1)

                    def vw_(u):
                        j, g = u // G, u % G
                        if u >= 2:
                            wait(pool, pe_unit, at, u - 2, "state")
                        else:
                            wait(pool, pe_qkT, at, NB - 1)
                            wait(pool, vec_rows, at, 0, "factors")
                            wait(pool, act_v, at, NB - 1)
                        c = (j * H + g * HG) * VS
                        f = j * RW + 32 + g * HG
                        pool.tensor_tensor(vw[:, u % 2, :, :], va[:, c:c + HG * VS].rearrange("p (h n) -> p h n", h=HG),
                                           rn[:, f:f + HG].unsqueeze(2).to_broadcast([P, HG, VS]), ALU.mult)\
                            .then_inc(pool_vw.sem, 1)

                    def x1_root(i):
                        wait(pool, vec_x1, at, i, "ms2")
                        root(rs[:, i:i + 1], ve[:, i:i + 1], 1, pool_x1)

                    mx_(0)
                    for t in range(NF):
                        slot = (half * NT + t) % 2
                        if t:
                            hid(at, t - 1)
                        if t in (2, 4, 6, 8):
                            wait(pool, vec_norm, at, t // 2 - 1, "mean")
                            root(rh[:], sm[:], H, pool_norm)
                        if t < UNITS:
                            vw_(t)
                        if t in (9, 10):
                            x1_root(0 if t == 9 else 3)
                        w_gu(at, t + 1, 1 - slot)
                        if t == 9:
                            x1_root(1)
                        w_dn(at, t, slot)
                        if t == 9:
                            x1_root(2)
                        if t in (1, 3, 5):
                            mx_(t // 2 + 1)
                    with pool.Fori(0, LOOPED // 2) as i:
                        for q in range(2):
                            t = i * 2 + (NF + q)
                            slot = (half * NT + NF + q) % 2
                            hid(at, t + -1)
                            w_gu(at, t + 1, 1 - slot)
                            w_dn(at, t, slot)
                    for t in range(NF + LOOPED, NT):
                        slot = (half * NT + t) % 2
                        hid(at, t - 1)
                        w_gu(at, t + 1, 1 - slot)
                        if t == NF + LOOPED + 1:
                            ln_root(at)
                        if t == NF + LOOPED + 2:
                            ln_root1(at, 1 - half)
                        w_dn(at, t, slot)
                    hid(at, NT - 1)


_INS = ["x", "w_attn", "w_gates", "norm1", "b_gates", "mh_w", "norm2", "w_gu", "w_dn", "lut", "idx"]


def kernel(L0_attn_x, L0_attn_norm1_w, L0_attn_wq, L0_attn_wk, L0_attn_wv, L0_attn_w_ig, L0_attn_b_ig, L0_attn_w_fg,
           L0_attn_b_fg, L0_attn_w_og, L0_attn_mh_w, L0_attn_w_out, L0_attn_norm2_w, L0_attn_w_gate, L0_attn_w_up,
           L0_attn_w_down, L0_ffn_lut, L0_ffn_gate_idx, L0_ffn_up_idx, L0_ffn_down_idx):
    import concourse.bacc as bacc
    from concourse.bass_utils import run_bass_kernel_spmd

    def rows_on_partitions(w):
        w = np.asarray(w)
        return w.reshape(-1, P, w.shape[1]).transpose(1, 0, 2)

    def column_tiles(w, n):
        return rows_on_partitions(w).reshape(P, KT, n, P).transpose(2, 0, 1, 3)

    def padded(i):
        i = np.asarray(i)
        return np.concatenate([i, np.zeros((INTER_PAD - INTER, i.shape[1]), i.dtype)])

    def all_partitions(v):
        return np.repeat(np.asarray(v).reshape(1, -1), P, 0)

    qk = np.concatenate([np.asarray(L0_attn_wq), np.asarray(L0_attn_wk)], 1)
    attn = [rows_on_partitions(w).reshape(P, 2, 2 * D).transpose(1, 0, 2)
            for w in (qk, L0_attn_wv, L0_attn_w_og, L0_attn_w_out)]
    gu = [column_tiles(w, NM).reshape(NM, P, KT * P) for w in (L0_attn_w_gate, L0_attn_w_up)]
    ix = [column_tiles(padded(i).T, NF).reshape(NF, P, KT * P) for i in (L0_ffn_gate_idx, L0_ffn_up_idx)]
    arrays = {
        "x": np.asarray(L0_attn_x).reshape(BATCH * SEQ, D),
        "w_attn": np.concatenate(attn),
        "w_gates": rows_on_partitions(np.concatenate([np.asarray(L0_attn_w_ig), np.asarray(L0_attn_w_fg)], 1)).reshape(P, -1),
        "norm1": np.asarray(L0_attn_norm1_w).reshape(KT, P).T,
        "b_gates": all_partitions(np.concatenate([np.asarray(L0_attn_b_ig), np.asarray(L0_attn_b_fg)])),
        "mh_w": all_partitions(L0_attn_mh_w),
        "norm2": np.asarray(L0_attn_norm2_w).reshape(KT, P).T,
        "w_gu": np.concatenate(gu, 2),
        "w_dn": np.asarray(L0_attn_w_down).reshape(NM, P, D),
        "lut": all_partitions(L0_ffn_lut),
        "idx": np.concatenate(ix + [padded(np.asarray(L0_ffn_down_idx).T).reshape(NF, P, D)], 2),
    }
    arrays = {k: np.ascontiguousarray(v) for k, v in arrays.items()}
    nc = bacc.Bacc("TRN2", target_bir_lowering=False, num_devices=1, dynamic_dma_scratch_size=8192)
    args = [nc.dram_tensor(n, arrays[n].shape, mybir.dt.from_np(arrays[n].dtype), kind="ExternalInput").ap() for n in _INS]
    res = nc.dram_tensor("result", (BATCH * SEQ, D), mybir.dt.float32, kind="ExternalOutput").ap()
    program(nc, *args, res)
    r = run_bass_kernel_spmd(nc, [arrays], core_ids=[0])
    return np.asarray(r.results[0]["result"]).reshape(BATCH, SEQ, D)
```
